# Optimizing a Trainium2 kernel written in Bass

```python
import numpy as np
import jax
import jax.numpy as jnp

def _softmax(x, axis=-1):
    return jax.nn.softmax(x, axis=axis)

def _gelu(x):
    return jax.nn.gelu(x, approximate=True)

def _silu(x):
    return jax.nn.silu(x)

def _sigmoid(x):
    return jax.nn.sigmoid(x)

def _layernorm(x, axis=-1, eps=1e-05):
    m = jnp.mean(x, axis=axis, keepdims=True)
    v = jnp.var(x, axis=axis, keepdims=True)
    return (x - m) / jnp.sqrt(v + eps)

def _scatter_add(tgt, idx, src, axis=0):
    return tgt.at[idx].add(src)

def _segment_sum(src, seg, n):
    return jax.ops.segment_sum(src, seg, n)
kernel_name = 'mk_gnn_ffn_d1_gnn_r8_c691b1'

def setup_inputs(seed: int=0):
    np.random.seed(seed)
    _w = jnp.asarray

    def _rec_inputs():
        import jax
        import jax.numpy as jnp
        _gk = jax.random.key(seed)
        x = -0.0003713 + 1 * jax.random.normal(jax.random.fold_in(_gk, 1), (6250, 256), jnp.float32)
        _s = jax.random.randint(jax.random.fold_in(_gk, 2), (50000,), 0, 6250, jnp.int32)
        _d = jax.random.randint(jax.random.fold_in(_gk, 3), (50000,), 0, 6250, jnp.int32)
        _loop = jnp.arange(6250, dtype=jnp.int32)
        src = jnp.concatenate([_s, _d, _loop])
        dst = jnp.concatenate([_d, _s, _loop])
        _o = jnp.argsort(dst, stable=True)
        src = src[_o]
        dst = dst[_o]
        edge_weight = jax.random.uniform(jax.random.fold_in(_gk, 12), (106250,), jnp.float32, 0.0, 0.999998)
        return (x, src, dst, edge_weight)
    x, src, dst, edge_weight = _rec_inputs()

    def _L0_gnn_setup():
        import jax, jax.numpy as jnp
        import numpy as np
        N_NODES = 6250
        N_EDGES = 100000
        IN_F = 256
        OUT_F = 64
        HEADS = 4
        NEG_SLOPE = 0.2
        key = jax.random.key(seed)
        ks = jax.random.split(key, 6)
        x = jax.random.normal(ks[0], (N_NODES, IN_F), dtype=jnp.float32)
        edge_index = jax.random.randint(ks[1], (2, N_EDGES), 0, N_NODES, dtype=jnp.int32)
        edge_weight = jax.random.uniform(ks[2], (N_EDGES,), dtype=jnp.float32)
        gain = float(np.sqrt(2.0 / (1.0 + NEG_SLOPE ** 2)))
        w_bound = gain * np.sqrt(6.0 / (IN_F + OUT_F))
        a_bound = gain * np.sqrt(6.0 / (OUT_F + 1))
        W = jax.random.uniform(ks[3], (HEADS, IN_F, OUT_F), minval=-w_bound, maxval=w_bound, dtype=jnp.float32)
        a_src = jax.random.uniform(ks[4], (HEADS, OUT_F, 1), minval=-a_bound, maxval=a_bound, dtype=jnp.float32)
        a_dst = jax.random.uniform(ks[5], (HEADS, OUT_F, 1), minval=-a_bound, maxval=a_bound, dtype=jnp.float32)
        return {'x': x, 'edge_index': edge_index, 'edge_weight': edge_weight, 'W': W, 'a_src': a_src, 'a_dst': a_dst}
    _L0_gnn_all = _L0_gnn_setup()
    _L0_gnn_in = {k: v for k, v in _L0_gnn_all.items() if k in ('W', 'a_src', 'a_dst')}
    del _L0_gnn_all

    def _L0_ffn_setup():
        import jax, jax.numpy as jnp
        import numpy as np
        E, D, H, TOP_K = (6, 256, 256, 2)
        ROUTER_H = D // 2
        key = jax.random.key(seed)
        ks = jax.random.split(key, 12)
        s = 1.0 / np.sqrt(D)
        sh = 1.0 / np.sqrt(H)
        sr = 1.0 / np.sqrt(ROUTER_H)
        return {'features': jax.random.normal(ks[0], (8, 512, D), dtype=jnp.float32), 'router_w1': jax.random.uniform(ks[1], (D, ROUTER_H), jnp.float32, -s, s), 'router_b1': jnp.zeros((ROUTER_H,), jnp.float32), 'router_w2': jax.random.uniform(ks[2], (ROUTER_H, E), jnp.float32, -sr, sr), 'router_b2': jnp.zeros((E,), jnp.float32), 'expert_w1': jax.random.uniform(ks[3], (E, D, H), jnp.float32, -s, s), 'expert_b1': jnp.zeros((E, H), jnp.float32), 'expert_w2': jax.random.uniform(ks[4], (E, H, H), jnp.float32, -sh, sh), 'expert_b2': jnp.zeros((E, H), jnp.float32), 'expert_w3': jax.random.uniform(ks[5], (E, H, D), jnp.float32, -sh, sh), 'expert_b3': jnp.zeros((E, D), jnp.float32)}
    _L0_ffn_all = _L0_ffn_setup()
    _L0_ffn_in = {k: v for k, v in _L0_ffn_all.items() if k in ('router_w1', 'router_b1', 'router_w2', 'router_b2', 'expert_w1', 'expert_b1', 'expert_w2', 'expert_b2', 'expert_w3', 'expert_b3')}
    del _L0_ffn_all
    return {'x': x, 'src': src, 'dst': dst, 'edge_weight': edge_weight, 'L0_gnn_W': _L0_gnn_in['W'], 'L0_gnn_a_src': _L0_gnn_in['a_src'], 'L0_gnn_a_dst': _L0_gnn_in['a_dst'], 'L0_ffn_router_w1': _L0_ffn_in['router_w1'], 'L0_ffn_router_b1': _L0_ffn_in['router_b1'], 'L0_ffn_router_w2': _L0_ffn_in['router_w2'], 'L0_ffn_router_b2': _L0_ffn_in['router_b2'], 'L0_ffn_expert_w1': _L0_ffn_in['expert_w1'], 'L0_ffn_expert_b1': _L0_ffn_in['expert_b1'], 'L0_ffn_expert_w2': _L0_ffn_in['expert_w2'], 'L0_ffn_expert_b2': _L0_ffn_in['expert_b2'], 'L0_ffn_expert_w3': _L0_ffn_in['expert_w3'], 'L0_ffn_expert_b3': _L0_ffn_in['expert_b3']}

def reference(x, src, dst, edge_weight, L0_gnn_W, L0_gnn_a_src, L0_gnn_a_dst, L0_ffn_router_w1, L0_ffn_router_b1, L0_ffn_router_w2, L0_ffn_router_b2, L0_ffn_expert_w1, L0_ffn_expert_b1, L0_ffn_expert_w2, L0_ffn_expert_b2, L0_ffn_expert_w3, L0_ffn_expert_b3):
    import jax
    import jax.numpy as jnp

    def _L0_gnn_ref(x, edge_index, edge_weight, W, a_src, a_dst):
        import jax, jax.numpy as jnp
        import numpy as np
        N_NODES = 6250
        N_EDGES = 100000
        IN_F = 256
        OUT_F = 64
        HEADS = 4
        NEG_SLOPE = 0.2
        num_nodes = x.shape[0]
        h = jnp.einsum('ni,hio->hno', x, W)
        attn_src = jnp.einsum('hno,hod->hn', h, a_src)
        attn_dst = jnp.einsum('hno,hod->hn', h, a_dst)
        src_idx, dst_idx = (edge_index[0], edge_index[1])
        e = attn_src[:, src_idx] + attn_dst[:, dst_idx]
        e = jnp.where(e >= 0, e, NEG_SLOPE * e)
        e = e * edge_weight[None, :]
        e_exp = jnp.exp(e - jnp.max(e))
        denom = jax.ops.segment_sum(e_exp.T, dst_idx, num_segments=num_nodes).T
        alpha = e_exp / (denom[:, dst_idx] + 1e-10)
        msg = h[:, src_idx] * alpha[..., None]
        out = jax.vmap(lambda m: jax.ops.segment_sum(m, dst_idx, num_segments=num_nodes))(msg)
        return jnp.transpose(out, (1, 0, 2)).reshape(num_nodes, HEADS * OUT_F)

    def _L0_ffn_ref(features, router_w1, router_b1, router_w2, router_b2, expert_w1, expert_b1, expert_w2, expert_b2, expert_w3, expert_b3):
        import jax, jax.numpy as jnp
        import numpy as np
        E, D, H, TOP_K = (6, 256, 256, 2)
        ROUTER_H = D // 2
        rh = jax.nn.relu(features @ router_w1 + router_b1)
        expert_logits = jax.nn.softmax(rh @ router_w2 + router_b2, axis=-1)
        top_w, top_i = jax.lax.top_k(expert_logits, TOP_K)
        routing_weights = jax.nn.softmax(top_w, axis=-1)
        h1 = jax.nn.relu(jnp.einsum('bsd,edh->bseh', features, expert_w1) + expert_b1)
        h2 = jax.nn.relu(jnp.einsum('bseh,ehf->bsef', h1, expert_w2) + expert_b2)
        expert_out = jnp.einsum('bsef,efo->bseo', h2, expert_w3) + expert_b3
        sel = jnp.take_along_axis(expert_out, top_i[:, :, :, None], axis=2)
        combined = jnp.sum(sel * routing_weights[..., None], axis=2)
        return combined
    edge_index = jnp.stack([src, dst])
    x = x + _L0_gnn_ref(_layernorm(x, axis=-1), edge_index, edge_weight, L0_gnn_W, L0_gnn_a_src, L0_gnn_a_dst)
    x = x + _L0_ffn_ref(_layernorm(x, axis=-1)[None], L0_ffn_router_w1, L0_ffn_router_b1, L0_ffn_router_w2, L0_ffn_router_b2, L0_ffn_expert_w1, L0_ffn_expert_b1, L0_ffn_expert_w2, L0_ffn_expert_b2, L0_ffn_expert_w3, L0_ffn_expert_b3)[0]
    return x

_drawn_inputs = setup_inputs


def setup_inputs(seed=0):
    import zlib

    import numpy as np

    out = dict(_drawn_inputs(seed))
    spreads = {'L0_ffn_router_b1': (0.0, 0.298),
     'L0_ffn_router_b2': (0.0, 0.1),
     'L0_ffn_expert_b1': (0.0, 0.8),
     'L0_ffn_expert_b2': (0.0, 0.421),
     'L0_ffn_expert_b3': (0.0, 0.1)}
    factors = {}
    for name, (base, spread) in spreads.items():
        noise = np.random.default_rng([zlib.crc32(name.encode()), seed]).standard_normal(out[name].shape)
        drawn = base * np.exp(spread * noise) if base else spread * noise
        out[name] = jnp.asarray(drawn.astype(out[name].dtype))
    for name, factor in factors.items():
        out[name] = (out[name] * factor).astype(out[name].dtype)
    return out
```

```python
import numpy as np
from contextlib import ExitStack

import concourse.bass as bass
from concourse import mybir

FP32 = mybir.dt.float32
INT32 = mybir.dt.int32
UINT32 = mybir.dt.uint32
ALU = mybir.AluOpType
ACT = mybir.ActivationFunctionType
AX = mybir.AxisListType

P = 128
NODES, D = 6250, 256
HEADS, HEAD_F = 4, 64
EDGES = 106250
EXPERTS, HIDDEN, ROUTER_H = 6, 256, 128
KC = D // P
BLOCKS = -(-NODES // P)
LAST_NODES = NODES - (BLOCKS - 1) * P
FULL_TILES = EDGES // P
EDGE_TILES = FULL_TILES + 2
GROUP = 8
SLOTS = -(-(FULL_TILES + 1 + BLOCKS - 1) // GROUP) * GROUP
GROUPS = SLOTS // GROUP
SLOT_CHUNKS = -(-SLOTS // P)
PAD_NODE = 1 << 20
ROW = D + HEADS
NROW = ROW + HEADS
ACOL = 2 * HEADS + 1
EPS = 1e-5
SLOPE = 0.2
DEN_EPS = 1e-10
FAR = 1e30
RING = 4
SRING = 4
STEPT = 7
CHUNK = 4


class Queue:

    def __init__(self, sem):
        self.sem, self.count, self.steps, self.seen = sem, 0, [], {}

    def wait(self, *marks):
        for sem, value in marks:
            if self.seen.get(id(sem), 0) < value:
                self.seen[id(sem)] = value
                self.steps.append(lambda e, s=sem, v=value: e.wait_ge(s, v))

    def run(self, make, *marks):
        self.wait(*marks)
        self.count += 1
        self.steps.append(lambda e: make(e).then_inc(self.sem, 1))
        return self.sem, self.count

    def send(self, make, sem, total, *marks):
        self.wait(*marks)
        total[0] += 16
        self.steps.append(lambda e: make(e).then_inc(sem, 16))
        return sem, total[0]

    def quiet(self, make, *marks):
        self.wait(*marks)
        self.steps.append(make)

    def replay(self, e):
        for step in self.steps:
            step(e)


def gnn_experts_kernel(nc, x, src, dst, edge_w, gnn_w, a_src, a_dst, rw1, rb1, rw2, rb2,
                       w1, b1, w2, b2, w3, b3, out):
    ctx = ExitStack()
    with ctx:
        ctx.enter_context(nc.allow_non_contiguous_dma(reason="tile ends and biases"))

        def sb(name, shape, dt=FP32):
            return ctx.enter_context(nc.sbuf_tensor(name, shape, dt))

        def psum(name):
            return ctx.enter_context(nc.psum_tensor(name, [P, 512], FP32))

        def sem(name):
            return ctx.enter_context(nc.semaphore(name))

        table = nc.dram_tensor("table", [NODES, ROW], FP32).ap()

        big = sb("big", [P, BLOCKS * D])
        x_all = big[:, :].rearrange("p (m d) -> p m d", d=D)
        WSZ = EXPERTS * KC * HIDDEN
        w_exp = [big[:, n * WSZ:(n + 1) * WSZ].rearrange("p (e k f) -> p e k f", e=EXPERTS, k=KC)
                 for n in range(3)]
        rw1_sb = big[:, 3 * WSZ:3 * WSZ + KC * ROUTER_H].rearrange("p (k f) -> p k f", k=KC)
        node = sb("node", [P, BLOCKS, NROW])
        gath = sb("gath", [P, RING * GROUP, ROW])
        sel = sb("sel", [P, SRING * GROUP, P])
        selT = sb("selT", [P, 2 * GROUP, P])
        srcT = sb("srcT", [P, SLOT_CHUNKS * P], INT32)
        dstT = sb("dstT", [P, SLOT_CHUNKS * P])
        wT = sb("wT", [P, SLOT_CHUNKS * P])
        dtab = sb("dtab", [P, BLOCKS, ACOL])
        wcat = sb("wcat", [P, KC, NROW])
        ident = sb("ident", [P, P])
        ones = sb("ones", [P, P])
        iota_row = sb("iota_row", [P, P])
        iota_i = sb("iota_i", [P, P], INT32)
        zeros = sb("zeros", [P, ROW])
        avec = sb("avec", [P, 2, D])
        small = sb("small", [P, 512])
        stats = sb("stats", [P, 4, 6])
        mv = sb("mv", [P, BLOCKS, 2])
        rstd = sb("rstd", [P, BLOCKS])
        xn = sb("xn", [P, 3, D])
        xnT = sb("xnT", [P, 2, D])
        z_t = sb("z_t", [P, 6, GROUP * HEADS])
        mask = sb("mask", [P, 2, GROUP])
        run_max = sb("run_max", [P, GROUP * HEADS])
        slot_i = sb("slot_i", [P, SLOT_CHUNKS], INT32)
        next_start = sb("next_start", [1, 64], INT32)
        blk_work = sb("blk_work", [P, SLOT_CHUNKS, BLOCKS])
        bound_in = sb("bound_in", [P, 2 * HEADS + 2])
        bound = sb("bound", [P, 2 * HEADS + 2])
        mx = sb("mx", [P, 2])
        b1_sb = sb("b1_sb", [P, EXPERTS, KC])
        b2_sb = sb("b2_sb", [P, EXPERTS, KC])
        b3_sb = sb("b3_sb", [EXPERTS, D])
        rb1_sb = sb("rb1_sb", [P, 1])
        rw2_sb = sb("rw2_sb", [P, EXPERTS])
        rb2_sb = sb("rb2_sb", [1, EXPERTS])

        gflat = gath[:, :, :].rearrange("p s r -> p (s r)")
        TOK = CHUNK * P
        xfT = gflat[:, 0:KC * TOK].rearrange("p (k t) -> p k t", k=KC)
        h1T = [gflat[:, (2 + 4 * n) * TOK:(4 + 4 * n) * TOK].rearrange("p (k t) -> p k t", k=KC) for n in range(2)]
        h2T = [gflat[:, (4 + 4 * n) * TOK:(6 + 4 * n) * TOK].rearrange("p (k t) -> p k t", k=KC) for n in range(2)]
        rhT = gflat[:, 10 * TOK:11 * TOK]
        sflat = sel[:, :, :].rearrange("p s r -> p (s r)")
        x_in = sflat[:, 0:2 * CHUNK * D].rearrange("p (b t d) -> p b t d", b=2, t=CHUNK)
        xf = sflat[:, 2 * CHUNK * D:3 * CHUNK * D].rearrange("p (t d) -> p t d", t=CHUNK)

        bank = [psum(f"bank{i}") for i in range(8)]

        s_dve, s_act, s_pe, s_pool = sem("s_dve"), sem("s_act"), sem("s_pe"), sem("s_pool")
        s_x = [sem(f"s_x{n}") for n in range(2)]
        s_par, s_tab, s_slot, s_w, s_out = sem("s_par"), sem("s_tab"), sem("s_slot"), sem("s_w"), sem("s_out")
        s_last = sem("s_last")
        s_row = [sem(f"s_row{n}") for n in range(RING)]
        s_agg = sem("s_agg")
        s_copied = sem("s_copied")
        s_free = sem("s_free")
        tot = {}

        dve, act, pe, pool, sp = (Queue(s) for s in (s_dve, s_act, s_pe, s_pool, None))

        def count(s):
            return tot.setdefault(id(s), [0])

        d_last = small[:, 0:SLOT_CHUNKS].bitcast(INT32)
        dst_rows = dst.rearrange("(t e) -> t e", e=P)
        pad_set = dve.run(lambda e: e.memset(d_last, PAD_NODE))
        FULL_K = EDGE_TILES // P
        got_last = sp.send(lambda e: e.dma_start(
            d_last[:, 0:FULL_K], dst_rows[0:FULL_K * P, P - 1:P].rearrange("(k p) o -> p (k o)", p=P)),
            s_last, count(s_last), pad_set)
        got_last = sp.send(lambda e: e.dma_start(
            d_last[0:EDGE_TILES - FULL_K * P, FULL_K:FULL_K + 1], dst_rows[FULL_K * P:EDGE_TILES, P - 1:P]),
            s_last, count(s_last))
        for k in range(KC):
            got_par = sp.send(lambda e, k=k: e.dma_start(
                wcat[:, k, 0:D].rearrange("p (h o) -> p h o", h=HEADS),
                gnn_w[:, k * P:(k + 1) * P, :].rearrange("h p o -> p h o")), s_par, count(s_par))
        for n, a in enumerate((a_src, a_dst)):
            got_par = sp.send(lambda e, n=n, a=a: e.dma_start(
                avec[:, n, :], a.rearrange("h o u -> (h o u)").partition_broadcast(P)), s_par, count(s_par))
        tail_zero = dve.run(lambda e: e.memset(x_all[:, BLOCKS - 1, :], 0.0))
        got_x = []
        for n in range(BLOCKS // STEPT):
            lo, hi = n * STEPT, (n + 1) * STEPT
            full = min(hi, BLOCKS - 1)
            s = s_x[n % 2]
            if n >= 2:
                sp.wait(got_x[n - 2])
            mark = sp.send(lambda e, lo=lo, full=full: e.dma_start(
                x_all[:, lo:full, :], x[lo * P:full * P, :].rearrange("(m p) d -> p m d", p=P)), s, count(s))
            if hi == BLOCKS:
                mark = sp.send(lambda e: e.dma_start(
                    x_all[0:LAST_NODES, BLOCKS - 1, :], x[(BLOCKS - 1) * P:NODES, :]), s, count(s), tail_zero)
            got_x.append(mark)

        c0 = pool.run(lambda e: e.iota(iota_i[:, :], pattern=[[1, P]], base=0, channel_multiplier=0))
        c1 = pool.run(lambda e: e.iota(slot_i[:, :], pattern=[[P, SLOT_CHUNKS]], base=0, channel_multiplier=1))
        c2 = pool.run(lambda e: e.memset(ones[:, :], 1.0))
        c3 = pool.run(lambda e: e.memset(ident[:, :], 0.0))
        c4 = pool.run(lambda e: e.affine_select(out=ident[:, :], in_=ident[:, :], compare_op=ALU.not_equal, fill=1.0,
                                                base=0, pattern=[[-1, P]], channel_multiplier=1), c3)
        iota_ok = dve.run(lambda e: e.tensor_copy(iota_row[:, :], iota_i[:, :]), c0)
        dve.run(lambda e: e.memset(zeros[:, :], 0.0))
        const_ok = dve.run(lambda e: e.memset(run_max[:, :], -FAR))

        lastf = small[:, 8:8 + SLOT_CHUNKS]
        slotf = small[:, 16:16 + SLOT_CHUNKS]
        blk_slot = small[:, 24:24 + SLOT_CHUNKS]
        base_slot = small[:, 32:32 + SLOT_CHUNKS]
        tilef = small[:, 40:40 + SLOT_CHUNKS]
        tile_slot = small[:, 48:48 + SLOT_CHUNKS].bitcast(INT32)
        first_node = small[:, 64:64 + BLOCKS]
        start = small[:, 128:128 + BLOCKS]
        shape3 = [P, SLOT_CHUNKS, BLOCKS]
        a0 = dve.run(lambda e: e.tensor_copy(lastf, d_last), got_last)
        a1 = dve.run(lambda e: e.tensor_scalar(first_node, iota_row[:, 0:BLOCKS], float(P), None, ALU.mult), iota_ok)
        a1b = dve.run(lambda e: e.tensor_copy(slotf, slot_i[:, :]), c1)
        a2 = dve.run(lambda e: e.tensor_tensor(blk_work[:, :, :], first_node.unsqueeze(1).broadcast_to(shape3),
                                               lastf.unsqueeze(2).broadcast_to(shape3), ALU.is_gt), a0, a1)
        for k in range(SLOT_CHUNKS):
            m = pe.run(lambda e, k=k: e.matmul(bank[0][:, 0:BLOCKS], ones[:, :], blk_work[:, k, :],
                                               start=(k == 0), stop=(k == SLOT_CHUNKS - 1)), a2, c2)
        a3 = dve.run(lambda e: e.tensor_tensor(start, bank[0][:, 0:BLOCKS], iota_row[:, 0:BLOCKS], ALU.add), m)
        a4 = dve.run(lambda e: e.tensor_tensor(blk_work[:, :, :], start.unsqueeze(1).broadcast_to(shape3),
                                               slotf.unsqueeze(2).broadcast_to(shape3), ALU.is_le), a3, a1b)
        next_ok = dve.run(lambda e: e.tensor_copy(next_start[0:1, 0:BLOCKS - 1], small[0:1, 129:128 + BLOCKS]), a3)
        never = dve.run(lambda e: e.memset(next_start[0:1, BLOCKS - 1:64], 1 << 20))
        a5 = dve.run(lambda e: e.tensor_reduce(blk_slot, blk_work[:, :, 1:BLOCKS], AX.X, ALU.add), a4)
        a6 = dve.run(lambda e: e.tensor_scalar(base_slot, blk_slot, float(P), None, ALU.mult), a5)
        a7 = dve.run(lambda e: e.tensor_tensor(tilef, slotf, blk_slot, ALU.subtract), a5)
        a8 = dve.run(lambda e: e.tensor_scalar(tile_slot, tilef, float(EDGE_TILES - 1), None, ALU.min), a7)

        stage = [sel[:, 8 * n:8 * n + SLOT_CHUNKS, :] for n in range(3)]
        stagef = sel[:, 24:24 + SLOT_CHUNKS, :]
        tables = [src.rearrange("(t e) -> t e", e=P), dst_rows, edge_w.rearrange("(t e) -> t e", e=P)]
        for n in (1, 0, 2):
            for k in range(SLOT_CHUNKS):
                dt = FP32 if n == 2 else INT32
                dstv = stage[n][:, k, :] if n == 2 else stage[n][:, k, :].bitcast(INT32)
                slots_in = pool.send(lambda e, n=n, k=k, dstv=dstv: e.indirect_dma_start(
                    out=dstv, out_offset=None, in_=tables[n],
                    in_offset=bass.IndirectOffsetOnAxis(ap=tile_slot[:, k:k + 1], axis=0)),
                    s_slot, count(s_slot), a8)

        for n in range(2):
            for k in range(KC):
                prod = xn[:, 0, :]
                b0 = dve.run(lambda e, n=n, k=k: e.tensor_tensor(xn[:, 0, :], wcat[:, k, 0:D], avec[:, n, :], ALU.mult),
                             got_par, (s_dve, dve.count))
                wcat_ok = dve.run(lambda e, n=n, k=k: e.tensor_reduce(
                    wcat[:, k, D + n * HEADS:D + (n + 1) * HEADS],
                    xn[:, 0, :].rearrange("p (h o) -> p h o", h=HEADS), AX.X, ALU.add), b0)

        def layer_norm_stats(views, lo, marks):
            for i, v in enumerate(views):
                q = (lo + i) % 4
                t = dve.run(lambda e, v=v, q=q: e.bn_stats(stats[:, q, :], v), marks[i], (s_dve, dve.count))
                t = dve.run(lambda e, i=i, q=q: e.bn_aggr(mv[:, lo + i, :], stats[:, q, :]), t)
            hi = lo + len(views)
            t = dve.run(lambda e: e.tensor_scalar(rstd[:, lo:hi], mv[:, lo:hi, 1], EPS, None, ALU.add), t)
            t = act.run(lambda e: e.activation(rstd[:, lo:hi], rstd[:, lo:hi], ACT.Sqrt), t)
            return dve.run(lambda e: e.reciprocal(rstd[:, lo:hi], rstd[:, lo:hi]), t)

        turned = {}
        copied = {}
        projected = {}
        rows_out = {}
        stored = None
        for n in range(BLOCKS // STEPT):
            lo, hi = n * STEPT, (n + 1) * STEPT
            norm = layer_norm_stats([x_all[:, m, :] for m in range(lo, hi)], lo, [got_x[n]] * STEPT)
            for m in range(lo, hi):
                free = [turned[m - 3]] if m >= 3 else []
                t = dve.run(lambda e, m=m: e.tensor_scalar(xn[:, m % 3, :], x_all[:, m, :], mv[:, m, 0:1],
                                                           rstd[:, m:m + 1], ALU.subtract, ALU.mult),
                            norm, wcat_ok, *free)
                free = [copied[m - 2]] if m >= 2 else []
                for k in range(KC):
                    turned[m] = pe.run(lambda e, m=m, k=k: e.transpose(
                        bank[1 + m % 2][:, k * P:(k + 1) * P], xn[:, m % 3, k * P:(k + 1) * P], ident[:, :]),
                        t, c4, *free)
                free = [projected[m - 2]] if m >= 2 else []
                copied[m] = act.run(lambda e, m=m: e.activation(xnT[:, m % 2, :], bank[1 + m % 2][:, 0:D], ACT.Copy),
                                    turned[m], *free)
                free = [rows_out[m - 2]] if m >= 2 else []
                for k in range(KC):
                    projected[m] = pe.run(lambda e, m=m, k=k: e.matmul(
                        bank[3 + m % 2][:, 0:NROW], xnT[:, m % 2, k * P:(k + 1) * P], wcat[:, k, :],
                        start=(k == 0), stop=(k == KC - 1)), copied[m], wcat_ok, *free)
                rows_out[m] = act.run(lambda e, m=m: e.activation(node[:, m, :], bank[3 + m % 2][:, 0:NROW], ACT.Copy),
                                      projected[m])
            full = min(hi, BLOCKS - 1)
            stored = sp.send(lambda e, lo=lo, full=full: e.dma_start(
                table[lo * P:full * P, :].rearrange("(m p) r -> p m r", p=P), node[:, lo:full, 0:ROW]),
                s_tab, count(s_tab), rows_out[hi - 1])
        stored = sp.send(lambda e: e.dma_start(table[(BLOCKS - 1) * P:NODES, :], node[0:LAST_NODES, BLOCKS - 1, 0:ROW]),
                         s_tab, count(s_tab), rows_out[BLOCKS - 1])

        turn_ok, tcopy = None, {}
        fl = {}
        for n, target in ((1, dstT), (0, srcT), (2, wT)):
            for k in range(SLOT_CHUNKS):
                j = len(fl)
                if n == 1:
                    t = dve.run(lambda e, k=k: e.tensor_scalar(stagef[:, k, :], stage[1][:, k, :].bitcast(INT32),
                                                               base_slot[:, k:k + 1], None, ALU.subtract),
                                slots_in, a6)
                    view = stagef[:, k, :]
                elif n == 0:
                    t = dve.run(lambda e, k=k: e.tensor_copy(stage[1][:, k, :], stage[0][:, k, :].bitcast(INT32)),
                                slots_in, (s_dve, dve.count))
                    view = stage[1][:, k, :]
                else:
                    t, view = slots_in, stage[2][:, k, :]
                b = bank[5 + j % 2]
                t = pe.run(lambda e, b=b, view=view: e.transpose(b[:, 0:P], view, ident[:, :]), t, c4,
                           *([fl[j - 2]] if j >= 2 else []))
                fl[j] = act.run(lambda e, b=b, k=k, target=target: e.activation(
                    target[:, k * P:(k + 1) * P], b[:, 0:P], ACT.Copy), t)
        tables_ok = fl[len(fl) - 1]

        nm = rows_out[BLOCKS - 1]
        part = [node[:, :, D:ROW].rearrange("p m h -> p h m"), wT[:, :]]
        g = dve.run(lambda e: e.tensor_reduce(bound_in[:, 0:HEADS], part[0], AX.X, ALU.max), nm)
        g = dve.run(lambda e: e.tensor_reduce(bound_in[:, HEADS:2 * HEADS], part[0], AX.X, ALU.min), nm)
        g = dve.run(lambda e: e.tensor_reduce(bound_in[:, 8:9], part[1], AX.X, ALU.max), tables_ok)
        g = dve.run(lambda e: e.tensor_reduce(bound_in[:, 9:10], part[1], AX.X, ALU.min), tables_ok)
        g = dve.run(lambda e: e.tensor_scalar(bound_in[:, 4:8], bound_in[:, 4:8], -1.0, None, ALU.mult), g)
        g = dve.run(lambda e: e.tensor_scalar(bound_in[:, 9:10], bound_in[:, 9:10], -1.0, None, ALU.mult), g)
        g = pool.run(lambda e: e.partition_all_reduce(bound[:, :], bound_in[:, :], P, bass.bass_isa.ReduceOp.max), g)
        g = dve.run(lambda e: e.tensor_scalar(bound[:, 4:8], bound[:, 4:8], -1.0, None, ALU.mult), g)
        g = dve.run(lambda e: e.tensor_scalar(bound[:, 9:10], bound[:, 9:10], -1.0, None, ALU.mult), g)
        nshape = [P, BLOCKS, HEADS]
        zb = [small[:, 192 * n:192 * n + 196] for n in range(1)]
        hi_z = xn[:, 0, 0:BLOCKS * HEADS].rearrange("p (m h) -> p m h", h=HEADS)
        lo_z = xn[:, 1, 0:BLOCKS * HEADS].rearrange("p (m h) -> p m h", h=HEADS)
        shift = dtab[:, :, HEADS:2 * HEADS]
        for z, sl in ((hi_z, bound[:, 0:4]), (lo_z, bound[:, 4:8])):
            g = dve.run(lambda e, z=z, sl=sl: e.tensor_tensor(z, node[:, :, ROW:NROW],
                                                              sl.unsqueeze(1).broadcast_to(nshape), ALU.add),
                        g, turned[BLOCKS - 1])
            g = dve.run(lambda e, z=z: e.scalar_tensor_tensor(out=z, in0=z, scalar=SLOPE, in1=z,
                                                              op0=ALU.mult, op1=ALU.max), g)
        g = dve.run(lambda e: e.tensor_scalar(shift, hi_z, bound[:, 8:9], None, ALU.mult), g)
        for z, wcol in ((hi_z, 9), (lo_z, 8), (lo_z, 9)):
            g = dve.run(lambda e, z=z, wcol=wcol: e.scalar_tensor_tensor(
                out=shift, in0=z, scalar=bound[:, wcol:wcol + 1], in1=shift, op0=ALU.mult, op1=ALU.max), g)
        g = dve.run(lambda e: e.tensor_copy(dtab[:, :, 0:HEADS], node[:, :, ROW:NROW]), g)
        dtab_ok = dve.run(lambda e: e.memset(dtab[:, :, 2 * HEADS:ACOL], 1.0), g)

        def load_w(view, source):
            return sp.send(lambda e: e.dma_start(view, source), s_w, count(s_w), turned[BLOCKS - 1])
        for n, w in enumerate((w1, w2, w3)):
            for ex in range(EXPERTS):
                load_w(w_exp[n][:, ex, :, :], w[ex, :, :].rearrange("(k p) f -> p k f", p=P))
        load_w(rw1_sb, rw1.rearrange("(k p) f -> p k f", p=P))
        load_w(rw2_sb[:, :], rw2)
        load_w(rb1_sb[:, :], rb1.rearrange("(p o) -> p o", o=1))
        load_w(rb2_sb[:, :], rb2.rearrange("(o e) -> o e", o=1))
        load_w(b1_sb[:, :, :], b1.rearrange("e (k p) -> p e k", p=P))
        load_w(b2_sb[:, :, :], b2.rearrange("e (k p) -> p e k", p=P))
        w_ok = load_w(b3_sb[:, :], b3)

        acc, tr_bank, dp_bank = bank[0], [bank[1], bank[2]], [bank[3], bank[4]]
        opened = pe.run(lambda e: e.matmul(acc[:, 0:ROW], zeros[:, 0:P], zeros[:, :], start=True, stop=True,
                                           skip_group_check=True), const_ok, a3)
        act.wait(opened, const_ok, next_ok, never)
        act.quiet(lambda e: e.activation(acc[:, 0:ROW], zeros[:, :], ACT.Copy).then_inc(s_free, 1))
        pe.wait(next_ok, never, dtab_ok)

        regs = {}

        def start_registers(which):
            def make(e):
                block = e.alloc_register(f"{which}_block")
                nxt = e.alloc_register(f"{which}_next")
                e.reg_mov(block, 0)
                e.load(nxt, next_start[0:1, 0:1])
                regs[which] = (block, nxt)
            return make

        def advance(e, which):
            block, nxt = regs[which]
            e.reg_add(block, block, 1)
            now = e.snap(block, min_val=0, max_val=BLOCKS)
            e.load(nxt, next_start[0:1, bass.ds(now, 1)])
            return now

        pe.quiet(start_registers("part"))
        pe.quiet(start_registers("sum"))
        act.quiet(start_registers("out"))

        def rows_at(g):
            return (g % RING) * GROUP

        row_marks, sel_marks, selT_marks, part_marks, exp_marks, msg_marks, logit_marks = {}, {}, {}, {}, {}, {}, {}

        def gather(g):
            if g >= RING:
                pool.wait((s_agg, (g - RING + 1) * GROUP))
            for i in range(GROUP):
                slot = g * GROUP + i
                row_marks[g] = pool.send(lambda e, slot=slot, at=rows_at(g) + i: e.indirect_dma_start(
                    out=gath[:, at, :], out_offset=None, in_=table,
                    in_offset=bass.IndirectOffsetOnAxis(ap=srcT[:, slot:slot + 1], axis=0)),
                    s_row[g % RING], count(s_row[g % RING]), stored, tables_ok)

        def selection(g):
            at = (g % SRING) * GROUP
            free = [(s_agg, (g - SRING + 1) * GROUP)] if g >= SRING else []
            shp = [P, GROUP, P]
            sel_marks[g] = dve.run(lambda e: e.tensor_tensor(
                sel[:, at:at + GROUP, :], iota_row[:, :].unsqueeze(1).broadcast_to(shp),
                dstT[:, g * GROUP:(g + 1) * GROUP].unsqueeze(2).broadcast_to(shp), ALU.is_equal),
                tables_ok, *free)

        def destination_parts(g):
            half = GROUP // 2
            for h in range(2):
                n = 2 * g + h
                at, to = (g % SRING) * GROUP + h * half, (g % 2) * GROUP + h * half
                free = [selT_marks[n - 2]] if n >= 2 else [copied[BLOCKS - 1]]
                for i in range(half):
                    t = pe.run(lambda e, i=i, n=n, at=at: e.transpose(
                        tr_bank[n % 2][:, i * P:(i + 1) * P], sel[:, at + i, :], ident[:, :]),
                        sel_marks[g], *free)
                free = [part_marks[g - 2]] if g >= 2 else []
                selT_marks[n] = act.run(lambda e, n=n, to=to: e.activation(
                    selT[:, to:to + half, :].rearrange("p s r -> p (s r)"), tr_bank[n % 2][:, :], ACT.Copy),
                    t, *free)
            pe.wait(logit_marks[g - 2] if g >= 2 else rows_out[BLOCKS - 1])
            for h in range(2):
                for i in range(half):
                    slot = g * GROUP + h * half + i
                    if slot:
                        def follow(e, slot=slot):
                            with e.If_eq(regs["part"][1], slot):
                                advance(e, "part")
                        pe.quiet(follow)

                    def product(e, g=g, col=(h * half + i) * 16, to=(g % 2) * GROUP + h * half + i):
                        now = e.snap(regs["part"][0], min_val=0, max_val=BLOCKS - 1)
                        return e.matmul(dp_bank[g % 2][:, col:col + ACOL], selT[:, to, :],
                                        dtab[:, bass.ds(now, 1), :].rearrange("p a f -> p (a f)"),
                                        start=True, stop=True)
                    part_marks[g] = pe.run(product, selT_marks[2 * g + h])

        def logits(g):
            b = dp_bank[g % 2][:, 0:GROUP * 16].rearrange("p (s c) -> p s c", c=16)
            at = rows_at(g)
            z = [z_t[:, n, :].rearrange("p (s h) -> p s h", h=HEADS) for n in range(6)]
            q = 3 * (g % 2)
            shp = [P, GROUP, HEADS]
            w_cols = wT[:, g * GROUP:(g + 1) * GROUP].unsqueeze(2).broadcast_to(shp)
            mk = mask[:, g % 2, :]
            t0 = dve.run(lambda e: e.tensor_tensor(z[q], gath[:, at:at + GROUP, D:ROW], b[:, :, 0:HEADS], ALU.add),
                         row_marks[g], part_marks[g], *([exp_marks[g - 2]] if g >= 2 else []))
            t1 = dve.run(lambda e: e.tensor_scalar(mk, b[:, :, 2 * HEADS], FAR, -FAR, ALU.mult, ALU.add), part_marks[g])
            t2 = dve.run(lambda e: e.scalar_tensor_tensor(out=z[q + 1], in0=z[q], scalar=SLOPE, in1=z[q],
                                                          op0=ALU.mult, op1=ALU.max), t0)
            t3 = dve.run(lambda e: e.tensor_tensor(z[q], z[q + 1], w_cols, ALU.mult), t2)
            t4 = dve.run(lambda e: e.tensor_tensor(z[q + 1], z[q], mk.unsqueeze(2).broadcast_to(shp), ALU.add), t3, t1)
            dve.run(lambda e: e.tensor_tensor(run_max[:, :], run_max[:, :], z_t[:, q + 1, :], ALU.max), t4)
            logit_marks[g] = dve.run(lambda e: e.tensor_tensor(z[q + 2], z[q + 1], b[:, :, HEADS:2 * HEADS],
                                                               ALU.subtract), t4)
            exp_marks[g] = act.run(lambda e: e.activation(
                gath[:, at:at + GROUP, D:ROW], z[q + 2], ACT.Exp), logit_marks[g])

        def messages(g):
            half = GROUP // 2
            for h in range(2):
                at = rows_at(g) + h * half
                rows = gath[:, at:at + half, 0:D].rearrange("p s (h o) -> p s h o", h=HEADS)
                ex = gath[:, at:at + half, D:ROW].unsqueeze(3).broadcast_to([P, half, HEADS, HEAD_F])
                msg_marks[2 * g + h] = dve.run(lambda e, rows=rows, ex=ex: e.tensor_tensor(rows, rows, ex, ALU.mult),
                                               exp_marks[g])

        def add_up(g):
            half = GROUP // 2
            for i in range(GROUP):
                slot = g * GROUP + i
                if slot == 0:
                    pe.wait((s_free, 1))
                else:
                    def follow(e, slot=slot):
                        with e.If_eq(regs["sum"][1], slot):
                            now = advance(e, "sum")
                            e.wait_ge(s_free, now + 1)
                    pe.quiet(follow)
                pe.quiet(lambda e, i=i, g=g: e.matmul(
                    acc[:, 0:ROW], sel[:, (g % SRING) * GROUP + i, :], gath[:, rows_at(g) + i, :],
                    start=False, stop=False, skip_group_check=True).then_inc(s_agg, 1),
                    msg_marks[2 * g + i // half])

        def take_out(g):
            for i in range(GROUP):
                slot = g * GROUP + i

                def body(e, slot=slot):
                    e.wait_ge(s_agg, slot + 1)
                    now = e.snap(regs["out"][0], min_val=0, max_val=BLOCKS - 1)
                    e.activation(node[:, bass.ds(now, 1), 0:ROW].rearrange("p a f -> p (a f)"), acc[:, 0:ROW],
                                 ACT.Copy).then_inc(s_copied, 1)
                    e.wait_ge(s_copied, now + 1)
                    e.activation(acc[:, 0:ROW], zeros[:, :], ACT.Copy).then_inc(s_free, 1)

                def step(e, slot=slot, body=body):
                    if slot == SLOTS - 1:
                        body(e)
                    else:
                        with e.If_eq(regs["out"][1], slot + 1):
                            body(e)
                            advance(e, "out")
                act.quiet(step)

        act.wait(dtab_ok, stored)
        for g in range(-2, GROUPS + 1):
            if 0 <= g + 2 < GROUPS:
                gather(g + 2)
                selection(g + 2)
                destination_parts(g + 2)
            if 0 <= g + 1 < GROUPS:
                logits(g + 1)
            if 0 <= g < GROUPS:
                messages(g)
                add_up(g)
                take_out(g)
        blocks_out = (s_free, BLOCKS + 1)

        g = dve.run(lambda e: e.tensor_reduce(mx[:, 0:1], run_max[:, :], AX.X, ALU.max), (s_dve, dve.count))
        g = pool.run(lambda e: e.partition_all_reduce(mx[:, 1:2], mx[:, 0:1], P, bass.bass_isa.ReduceOp.max), g)
        eps_t = xn[:, 2, 0:BLOCKS * HEADS].rearrange("p (m h) -> p m h", h=HEADS)
        g = act.run(lambda e: e.activation(eps_t, shift, ACT.Exp, bias=mx[:, 1:2], scale=-1.0), g)
        g = dve.run(lambda e: e.scalar_tensor_tensor(out=eps_t, in0=eps_t, scalar=DEN_EPS, in1=node[:, :, D:ROW],
                                                     op0=ALU.mult, op1=ALU.add), g, blocks_out)
        rden = xn[:, 1, 0:BLOCKS * HEADS].rearrange("p (m h) -> p m h", h=HEADS)
        den_ok = dve.run(lambda e: e.reciprocal(rden, eps_t), g)

        T8 = [P, CHUNK, 8]
        probs, gate = sb("probs", T8), sb("gate", T8)
        top, topi, topf = sb("top", T8), sb("topi", T8, UINT32), sb("topf", T8)
        pick = sb("pick", T8)
        rt = sb("rt", [P, 4, CHUNK])
        gT = sb("gT", [8, CHUNK * P])
        probs_pad = dve.run(lambda e: e.memset(probs[:, :, :], -1.0))
        CHUNKS = -(-BLOCKS // CHUNK)
        h_bank, y_bank, tr2, small_bank = [bank[1], bank[2], bank[3]], [bank[4], bank[5]], bank[6], bank[7]
        n_h, n_y = [0], [0]
        h_free, y_free = {}, {}
        tr_free, sb_free = [blocks_out], [blocks_out]
        x1_done, chunk_out = {}, {}
        xfT_read, xf_read = [blocks_out], [blocks_out]
        last_out = [None]

        def experts(c):
            lo, hi = c * CHUNK, min((c + 1) * CHUNK, BLOCKS)
            nt = hi - lo
            N = nt * P
            buf = c % 2
            full = min(hi, BLOCKS - 1)
            xfree = [x1_done[c - 2]] if c >= 2 else [blocks_out]
            if full > lo:
                got = sp.send(lambda e, lo=lo, full=full, buf=buf: e.dma_start(
                    x_in[:, buf, 0:full - lo, :], x[lo * P:full * P, :].rearrange("(m p) d -> p m d", p=P)),
                    s_x[buf], count(s_x[buf]), *xfree)
            if hi == BLOCKS:
                z = dve.run(lambda e, buf=buf, at=full - lo: e.memset(x_in[:, buf, at, :], 0.0), *xfree)
                got = sp.send(lambda e, buf=buf, at=full - lo: e.dma_start(
                    x_in[0:LAST_NODES, buf, at, :], x[(BLOCKS - 1) * P:NODES, :]), s_x[buf], count(s_x[buf]), z)
            marks = []
            for m in range(lo, hi):
                view = node[:, m, 0:D].rearrange("p (h o) -> p h o", h=HEADS)
                t = dve.run(lambda e, m=m, view=view: e.tensor_tensor(
                    view, view, rden[:, m, :].unsqueeze(2).broadcast_to([P, HEADS, HEAD_F]), ALU.mult),
                    den_ok, blocks_out)
                marks.append(dve.run(lambda e, m=m, buf=buf, lo=lo: e.tensor_tensor(
                    node[:, m, 0:D], node[:, m, 0:D], x_in[:, buf, m - lo, :], ALU.add), t, got))
            x1_done[c] = marks[-1]
            norm = layer_norm_stats([node[:, m, 0:D] for m in range(lo, hi)], lo, marks)
            for m in range(lo, hi):
                t = dve.run(lambda e, m=m, lo=lo: e.tensor_scalar(xf[:, m - lo, :], node[:, m, 0:D], mv[:, m, 0:1],
                                                                  rstd[:, m:m + 1], ALU.subtract, ALU.mult),
                            norm, xf_read[0])
            for m in range(lo, hi):
                for k in range(KC):
                    t2 = pe.run(lambda e, m=m, k=k, lo=lo: e.transpose(
                        tr2[:, k * P:(k + 1) * P], xf[:, m - lo, k * P:(k + 1) * P], ident[:, :]), t, tr_free[0])
                tr_free[0] = act.run(lambda e, m=m, lo=lo: e.activation(
                    xfT[:, :, (m - lo) * P:(m - lo + 1) * P], tr2[:, 0:D].rearrange("p (k t) -> p k t", k=KC),
                    ACT.Copy), t2, xfT_read[0])
            xf_read[0] = t2
            xfT_ok = tr_free[0]

            def hidden(products, bias, target, marks, N=N):
                n = n_h[0]
                n_h[0] += 1
                b = h_bank[n % 3]
                for i, (l, r) in enumerate(products):
                    t = pe.run(lambda e, l=l, r=r, i=i, b=b: e.matmul(b[:, 0:N], l, r, start=(i == 0),
                                                                      stop=(i == len(products) - 1)),
                               *marks, h_free.get(n - 3, blocks_out))
                h_free[n] = act.run(lambda e, b=b: e.activation(target, b[:, 0:N], ACT.Relu, bias=bias), t)
                return h_free[n]

            rh_ok = hidden([(rw1_sb[:, k, :], xfT[:, k, 0:N]) for k in range(KC)], rb1_sb[:, 0:1], rhT[:, 0:N],
                           [xfT_ok, w_ok])
            for i in range(nt):
                pe.run(lambda e, i=i: e.matmul(small_bank[:, 8 * i:8 * i + EXPERTS], rhT[:, i * P:(i + 1) * P],
                                               rw2_sb[:, :], start=True, stop=False), rh_ok, sb_free[0])
                t = pe.run(lambda e, i=i: e.matmul(small_bank[:, 8 * i:8 * i + EXPERTS], ones[0:1, :],
                                                   rb2_sb[:, :], start=False, stop=True))
            s3 = [P, nt, EXPERTS]
            lg = small_bank[:, 0:8 * nt].rearrange("p (t c) -> p t c", c=8)[:, :, 0:EXPERTS]
            pv, gv, kv = (v[:, 0:nt, 0:EXPERTS] for v in (probs, gate, pick))

            def row(n, nt=nt):
                return rt[:, n, 0:nt]

            def wide(v, s3=s3):
                return v.unsqueeze(2).broadcast_to(s3)

            t = dve.run(lambda e: e.tensor_reduce(row(0), lg, AX.X, ALU.max), t, probs_pad, (s_dve, dve.count))
            t = dve.run(lambda e: e.tensor_tensor(pv, lg, wide(row(0)), ALU.subtract), t)
            sb_free[0] = t
            t = act.run(lambda e: e.activation(pv, pv, ACT.Exp), t)
            t = dve.run(lambda e: e.tensor_reduce(row(0), pv, AX.X, ALU.add), t)
            t = dve.run(lambda e: e.reciprocal(row(1), row(0)), t)
            t = dve.run(lambda e: e.tensor_tensor(pv, pv, wide(row(1)), ALU.mult), t)
            for i in range(nt):
                t = dve.run(lambda e, i=i: e.max(top[:, i, :], probs[:, i, :]), t)
                t = dve.run(lambda e, i=i: e.max_index(topi[:, i, :], top[:, i, :], probs[:, i, :]), t)
            t = dve.run(lambda e: e.tensor_copy(topf[:, 0:nt, 0:2], topi[:, 0:nt, 0:2]), t)
            t = dve.run(lambda e: e.tensor_tensor(row(0), top[:, 0:nt, 1], top[:, 0:nt, 0], ALU.subtract), t)
            t = act.run(lambda e: e.activation(row(1), row(0), ACT.Exp), t)
            t = dve.run(lambda e: e.tensor_scalar(row(0), row(1), 1.0, None, ALU.add), t)
            t = dve.run(lambda e: e.reciprocal(row(2), row(0)), t)
            t = dve.run(lambda e: e.tensor_tensor(row(3), row(1), row(2), ALU.mult), t)
            for j, target in ((0, gv), (1, kv)):
                t = dve.run(lambda e, j=j, target=target: e.tensor_tensor(
                    target, iota_row[:, 0:EXPERTS].unsqueeze(1).broadcast_to(s3), wide(topf[:, 0:nt, j]),
                    ALU.is_equal), t)
                t = dve.run(lambda e, j=j, target=target: e.tensor_tensor(target, target, wide(row(2 + j)), ALU.mult), t)
            gate_ok = dve.run(lambda e: e.tensor_tensor(gv, gv, kv, ALU.add), t)
            for i in range(nt):
                t = pe.run(lambda e, i=i: e.transpose(small_bank[0:EXPERTS, i * P:(i + 1) * P],
                                                      gate[:, i, 0:EXPERTS], ident[:, :]), gate_ok)
            gT_ok = act.run(lambda e: e.activation(gT[0:EXPERTS, 0:N], small_bank[0:EXPERTS, 0:N], ACT.Copy), t)
            sb_free[0] = gT_ok

            def output(products, i, scalar, marks, lo=lo):
                n = n_y[0]
                n_y[0] += 1
                b = y_bank[n % 2]
                for j, (l, r) in enumerate(products):
                    t = pe.run(lambda e, l=l, r=r, j=j, b=b: e.matmul(b[:, 0:D], l, r, start=(j == 0),
                                                                      stop=(j == len(products) - 1)),
                               *marks, y_free.get(n - 2, blocks_out))
                rows = node[:, lo + i, 0:D]
                y_free[n] = dve.run(lambda e, b=b: e.scalar_tensor_tensor(
                    out=rows, in0=b[:, 0:D], scalar=scalar, in1=rows, op0=ALU.mult, op1=ALU.add),
                    t, (s_dve, dve.count))
                return t, y_free[n]

            def layer1(ex):
                return [hidden([(w_exp[0][:, ex, k, f * P:(f + 1) * P], xfT[:, k, 0:N]) for k in range(KC)],
                               b1_sb[:, ex, f:f + 1], h1T[ex % 2][:, f, 0:N], [xfT_ok]) for f in range(KC)][-1]

            def layer2(ex, ready):
                return [hidden([(w_exp[1][:, ex, k, f * P:(f + 1) * P], h1T[ex % 2][:, k, 0:N]) for k in range(KC)],
                               b2_sb[:, ex, f:f + 1], h2T[ex % 2][:, f, 0:N], [ready]) for f in range(KC)][-1]

            def layer3(ex, ready):
                for i in range(nt):
                    t = output([(h2T[ex % 2][:, k, i * P:(i + 1) * P], w_exp[2][:, ex, k, :]) for k in range(KC)],
                               i, gate[:, i, ex:ex + 1], [ready, gate_ok])
                return t

            r1 = layer1(0)
            r2 = None
            for ex in range(EXPERTS):
                nxt = layer1(ex + 1) if ex + 1 < EXPERTS else None
                if nxt:
                    xfT_read[0] = (s_pe, pe.count)
                if r2:
                    layer3(ex - 1, r2)
                r2 = layer2(ex, r1)
                r1 = nxt
            for i in range(nt):
                output([(gT[0:EXPERTS, i * P:(i + 1) * P], b3_sb[:, :])], i, 1.0, [gT_ok])
            _, fin = layer3(EXPERTS - 1, r2)
            if full > lo:
                last_out[0] = sp.send(lambda e, lo=lo, full=full: e.dma_start(
                    out[lo * P:full * P, :].rearrange("(m p) d -> p m d", p=P), node[:, lo:full, 0:D]),
                    s_out, count(s_out), fin)
            if hi == BLOCKS:
                last_out[0] = sp.send(lambda e: e.dma_start(out[(BLOCKS - 1) * P:NODES, :],
                                                         node[0:LAST_NODES, BLOCKS - 1, 0:D]),
                                   s_out, count(s_out), fin)

        for c in range(CHUNKS):
            experts(c)
        sp.wait(last_out[0])

        block = ctx.enter_context(nc.Block())

        @block.sync
        def _(e):
            sp.replay(e)

        @block.gpsimd
        def _(e):
            pool.replay(e)

        @block.vector
        def _(e):
            dve.replay(e)

        @block.scalar
        def _(e):
            act.replay(e)

        @block.tensor
        def _(e):
            pe.replay(e)


def kernel(**inputs):
    import concourse.bacc as bacc
    from concourse.bass_utils import run_bass_kernel_spmd

    nc = bacc.Bacc("TRN2", target_bir_lowering=False, num_devices=1)
    padding = EDGE_TILES * P - EDGES
    fill = {"src": 0, "dst": PAD_NODE, "edge_weight": 0}
    arrays, args = {}, []
    for name in ("x", "src", "dst", "edge_weight", "L0_gnn_W", "L0_gnn_a_src", "L0_gnn_a_dst",
                 "L0_ffn_router_w1", "L0_ffn_router_b1", "L0_ffn_router_w2", "L0_ffn_router_b2",
                 "L0_ffn_expert_w1", "L0_ffn_expert_b1", "L0_ffn_expert_w2", "L0_ffn_expert_b2",
                 "L0_ffn_expert_w3", "L0_ffn_expert_b3"):
        a = np.ascontiguousarray(inputs[name])
        if name in fill:
            a = np.concatenate([a, np.full(padding, fill[name], a.dtype)])
        arrays[f"in_{name}"] = a
        args.append(nc.dram_tensor(f"in_{name}", a.shape, mybir.dt.from_np(a.dtype), kind="ExternalInput").ap())
    out = nc.dram_tensor("out_nodes", (NODES, D), FP32, kind="ExternalOutput").ap()
    gnn_experts_kernel(nc, *args, out)
    result = run_bass_kernel_spmd(nc, [arrays], core_ids=[0])
    return result.results[0]["out_nodes"]
```
